# Optimizing a Trainium2 kernel written in Bass

```python
import numpy as np
import jax
import jax.numpy as jnp

def _softmax(x, axis=-1):
    return jax.nn.softmax(x, axis=axis)

def _gelu(x):
    return jax.nn.gelu(x, approximate=True)

def _silu(x):
    return jax.nn.silu(x)

def _sigmoid(x):
    return jax.nn.sigmoid(x)

def _layernorm(x, axis=-1, eps=1e-05):
    m = jnp.mean(x, axis=axis, keepdims=True)
    v = jnp.var(x, axis=axis, keepdims=True)
    return (x - m) / jnp.sqrt(v + eps)

def _scatter_add(tgt, idx, src, axis=0):
    return tgt.at[idx].add(src)

def _segment_sum(src, seg, n):
    return jax.ops.segment_sum(src, seg, n)
kernel_name = 'mk_dlrm_tower_d1_rec_r8_bcf234'

def setup_inputs(seed: int=0):
    np.random.seed(seed)
    _w = jnp.asarray

    def _rec_inputs():
        import jax
        import jax.numpy as jnp
        _tk = jax.random.key(seed)
        ids = jnp.stack([jax.random.randint(jax.random.fold_in(_tk, 200 + f), (512,), 0, v, jnp.int32) for f, v in enumerate([125000, 12500, 12500, 1250, 1250, 1250, 1250, 1250, 1000, 1000, 12500, 1250, 12500, 1000, 12500, 1000, 1000, 1000, 12500, 1000, 12500, 1000, 12500, 1250, 1000, 1250])], axis=1)
        tbl_0 = 0.05 * jax.random.normal(jax.random.fold_in(_tk, 500 + 0), (125000, 128), jnp.float32)
        tbl_1 = 0.05 * jax.random.normal(jax.random.fold_in(_tk, 500 + 1), (12500, 128), jnp.float32)
        tbl_2 = 0.05 * jax.random.normal(jax.random.fold_in(_tk, 500 + 2), (12500, 128), jnp.float32)
        tbl_3 = 0.05 * jax.random.normal(jax.random.fold_in(_tk, 500 + 3), (1250, 128), jnp.float32)
        tbl_4 = 0.05 * jax.random.normal(jax.random.fold_in(_tk, 500 + 4), (1250, 128), jnp.float32)
        tbl_5 = 0.05 * jax.random.normal(jax.random.fold_in(_tk, 500 + 5), (1250, 128), jnp.float32)
        tbl_6 = 0.05 * jax.random.normal(jax.random.fold_in(_tk, 500 + 6), (1250, 128), jnp.float32)
        tbl_7 = 0.05 * jax.random.normal(jax.random.fold_in(_tk, 500 + 7), (1250, 128), jnp.float32)
        tbl_8 = 0.05 * jax.random.normal(jax.random.fold_in(_tk, 500 + 8), (1000, 128), jnp.float32)
        tbl_9 = 0.05 * jax.random.normal(jax.random.fold_in(_tk, 500 + 9), (1000, 128), jnp.float32)
        tbl_10 = 0.05 * jax.random.normal(jax.random.fold_in(_tk, 500 + 10), (12500, 128), jnp.float32)
        tbl_11 = 0.05 * jax.random.normal(jax.random.fold_in(_tk, 500 + 11), (1250, 128), jnp.float32)
        tbl_12 = 0.05 * jax.random.normal(jax.random.fold_in(_tk, 500 + 12), (12500, 128), jnp.float32)
        tbl_13 = 0.05 * jax.random.normal(jax.random.fold_in(_tk, 500 + 13), (1000, 128), jnp.float32)
        tbl_14 = 0.05 * jax.random.normal(jax.random.fold_in(_tk, 500 + 14), (12500, 128), jnp.float32)
        tbl_15 = 0.05 * jax.random.normal(jax.random.fold_in(_tk, 500 + 15), (1000, 128), jnp.float32)
        tbl_16 = 0.05 * jax.random.normal(jax.random.fold_in(_tk, 500 + 16), (1000, 128), jnp.float32)
        tbl_17 = 0.05 * jax.random.normal(jax.random.fold_in(_tk, 500 + 17), (1000, 128), jnp.float32)
        tbl_18 = 0.05 * jax.random.normal(jax.random.fold_in(_tk, 500 + 18), (12500, 128), jnp.float32)
        tbl_19 = 0.05 * jax.random.normal(jax.random.fold_in(_tk, 500 + 19), (1000, 128), jnp.float32)
        tbl_20 = 0.05 * jax.random.normal(jax.random.fold_in(_tk, 500 + 20), (12500, 128), jnp.float32)
        tbl_21 = 0.05 * jax.random.normal(jax.random.fold_in(_tk, 500 + 21), (1000, 128), jnp.float32)
        tbl_22 = 0.05 * jax.random.normal(jax.random.fold_in(_tk, 500 + 22), (12500, 128), jnp.float32)
        tbl_23 = 0.05 * jax.random.normal(jax.random.fold_in(_tk, 500 + 23), (1250, 128), jnp.float32)
        tbl_24 = 0.05 * jax.random.normal(jax.random.fold_in(_tk, 500 + 24), (1000, 128), jnp.float32)
        tbl_25 = 0.05 * jax.random.normal(jax.random.fold_in(_tk, 500 + 25), (1250, 128), jnp.float32)
        _rk = jax.random.fold_in(_tk, 7)
        r_dense_features = -0.000520686 + 1.00062 * jax.random.normal(jax.random.fold_in(_rk, 101), (512, 128), jnp.float32)
        W_top1 = 0.0405887 * jax.random.normal(jax.random.fold_in(_tk, 801), (607, 512), jnp.float32)
        W_top2 = 0.0441942 * jax.random.normal(jax.random.fold_in(_tk, 802), (512, 256), jnp.float32)
        W_top3 = 0.0625 * jax.random.normal(jax.random.fold_in(_tk, 803), (256, 1), jnp.float32)
        b_top1 = jnp.zeros((512,), jnp.float32)
        b_top2 = jnp.zeros((256,), jnp.float32)
        return (r_dense_features, ids, tbl_0, tbl_1, tbl_2, tbl_3, tbl_4, tbl_5, tbl_6, tbl_7, tbl_8, tbl_9, tbl_10, tbl_11, tbl_12, tbl_13, tbl_14, tbl_15, tbl_16, tbl_17, tbl_18, tbl_19, tbl_20, tbl_21, tbl_22, tbl_23, tbl_24, tbl_25, W_top1, b_top1, W_top2, b_top2, W_top3)
    r_dense_features, ids, tbl_0, tbl_1, tbl_2, tbl_3, tbl_4, tbl_5, tbl_6, tbl_7, tbl_8, tbl_9, tbl_10, tbl_11, tbl_12, tbl_13, tbl_14, tbl_15, tbl_16, tbl_17, tbl_18, tbl_19, tbl_20, tbl_21, tbl_22, tbl_23, tbl_24, tbl_25, W_top1, b_top1, W_top2, b_top2, W_top3 = _rec_inputs()

    def _L0_rec_setup():
        import jax, jax.numpy as jnp
        import numpy as np
        F = 26
        N = F + 1
        _TRIU_I, _TRIU_J = np.triu_indices(N, k=1)
        key = jax.random.key(seed)
        k1, k2 = jax.random.split(key)
        B, D = (2048, 128)
        dense_features = jax.random.normal(k1, (B, D), dtype=jnp.float32)
        sparse_features = jax.random.normal(k2, (B, F, D), dtype=jnp.float32)
        return {'dense_features': dense_features, 'sparse_features': sparse_features}
    _L0_rec_all = _L0_rec_setup()
    _L0_rec_in = {k: v for k, v in _L0_rec_all.items() if k in ()}
    del _L0_rec_all
    return {'r_dense_features': r_dense_features, 'ids': ids, 'tbl_0': tbl_0, 'tbl_1': tbl_1, 'tbl_2': tbl_2, 'tbl_3': tbl_3, 'tbl_4': tbl_4, 'tbl_5': tbl_5, 'tbl_6': tbl_6, 'tbl_7': tbl_7, 'tbl_8': tbl_8, 'tbl_9': tbl_9, 'tbl_10': tbl_10, 'tbl_11': tbl_11, 'tbl_12': tbl_12, 'tbl_13': tbl_13, 'tbl_14': tbl_14, 'tbl_15': tbl_15, 'tbl_16': tbl_16, 'tbl_17': tbl_17, 'tbl_18': tbl_18, 'tbl_19': tbl_19, 'tbl_20': tbl_20, 'tbl_21': tbl_21, 'tbl_22': tbl_22, 'tbl_23': tbl_23, 'tbl_24': tbl_24, 'tbl_25': tbl_25, 'W_top1': W_top1, 'b_top1': b_top1, 'W_top2': W_top2, 'b_top2': b_top2, 'W_top3': W_top3}

def reference(r_dense_features, ids, tbl_0, tbl_1, tbl_2, tbl_3, tbl_4, tbl_5, tbl_6, tbl_7, tbl_8, tbl_9, tbl_10, tbl_11, tbl_12, tbl_13, tbl_14, tbl_15, tbl_16, tbl_17, tbl_18, tbl_19, tbl_20, tbl_21, tbl_22, tbl_23, tbl_24, tbl_25, W_top1, b_top1, W_top2, b_top2, W_top3):
    import jax
    import jax.numpy as jnp

    def _L0_rec_ref(dense_features, sparse_features):
        import jax, jax.numpy as jnp
        import numpy as np
        F = 26
        N = F + 1
        _TRIU_I, _TRIU_J = np.triu_indices(N, k=1)
        combined = jnp.concatenate([dense_features[:, None, :], sparse_features], axis=1)
        interactions = jnp.einsum('bnd,bmd->bnm', combined, combined)
        interactions_flat = interactions[:, _TRIU_I, _TRIU_J]
        return jnp.concatenate([dense_features, interactions_flat], axis=1)
    e = jnp.stack([tbl_0[ids[:, 0]], tbl_1[ids[:, 1]], tbl_2[ids[:, 2]], tbl_3[ids[:, 3]], tbl_4[ids[:, 4]], tbl_5[ids[:, 5]], tbl_6[ids[:, 6]], tbl_7[ids[:, 7]], tbl_8[ids[:, 8]], tbl_9[ids[:, 9]], tbl_10[ids[:, 10]], tbl_11[ids[:, 11]], tbl_12[ids[:, 12]], tbl_13[ids[:, 13]], tbl_14[ids[:, 14]], tbl_15[ids[:, 15]], tbl_16[ids[:, 16]], tbl_17[ids[:, 17]], tbl_18[ids[:, 18]], tbl_19[ids[:, 19]], tbl_20[ids[:, 20]], tbl_21[ids[:, 21]], tbl_22[ids[:, 22]], tbl_23[ids[:, 23]], tbl_24[ids[:, 24]], tbl_25[ids[:, 25]]], axis=1)
    z = _L0_rec_ref(r_dense_features, e)
    z = z.reshape(z.shape[0], -1)
    h = jnp.concatenate([z, r_dense_features], axis=1)
    h = jnp.maximum(h @ W_top1 + b_top1, 0.0)
    h = jnp.maximum(h @ W_top2 + b_top2, 0.0)
    y = h @ W_top3
    return y

_drawn_inputs = setup_inputs


def setup_inputs(seed=0):
    import zlib

    import numpy as np

    out = dict(_drawn_inputs(seed))
    spreads = {'b_top1': (0.0, 0.1), 'b_top2': (0.0, 0.1)}
    factors = {}
    for name, (base, spread) in spreads.items():
        noise = np.random.default_rng([zlib.crc32(name.encode()), seed]).standard_normal(out[name].shape)
        drawn = base * np.exp(spread * noise) if base else spread * noise
        out[name] = jnp.asarray(drawn.astype(out[name].dtype))
    for name, factor in factors.items():
        out[name] = (out[name] * factor).astype(out[name].dtype)
    return out
```

```python
from contextlib import ExitStack

import concourse.bass as bass
from concourse import mybir

F32 = mybir.dt.float32
I32 = mybir.dt.int32
ALU = mybir.AluOpType
ACT = mybir.ActivationFunctionType

P = 128
Q = 32
NSPARSE = 26
NF = NSPARSE + 1
NSLOT = NF - 1
GS = 4
TF = 4


def dlrm_tower(nc, dense, ids, tables, w1, b1, w2, b2, w3, out):
    batch, _ = ids.shape
    nt = batch // P
    h1n = w1.shape[1]
    h2n = w2.shape[1]
    m1 = h1n // P
    m2 = h2n // P
    nc_pair = -(-NSLOT // 4)
    n_tg = -(-NF // TF)
    n_gram = P // GS
    gb = 8
    n_gb = n_gram // gb

    with ExitStack() as ctx:
        def sb(name, shape, dt=F32):
            return ctx.enter_context(nc.sbuf_tensor(name, shape, dt))

        def ps(name, shape):
            return ctx.enter_context(nc.psum_tensor(name, shape, F32))

        def sem(name):
            return ctx.enter_context(nc.semaphore(name))

        idx = sb("idx", [P, nt * NSPARSE], I32)
        ident = sb("ident", [P, P])
        dense_sb = sb("dense_sb", [P, nt, P])
        rows = sb("rows", [P, nt, NSPARSE, P])
        feat_T = sb("feat_T", [P, 2, P, Q])
        pairs = sb("pairs", [P, 2, nc_pair, P])
        w1_pair = sb("w1_pair", [P, nc_pair, h1n])
        w1_dense = sb("w1_dense", [P, 3, h1n])
        w2_sb = sb("w2_sb", [P, m1, h2n])
        vec_rows = sb("vec_rows", [m1 + 2 * m2, P])
        vec_T = sb("vec_T", [P, m1 + 2 * m2])
        b1_sb = vec_T[:, 0:m1]
        b2_sb = vec_T[:, m1:m1 + m2]
        w3_sb = vec_T[:, m1 + m2:m1 + 2 * m2]
        h1_T = sb("h1_T", [P, m1, P])
        h2_T = sb("h2_T", [P, m2, P])
        y_sb = sb("y_sb", [P, nt])

        ps_tp = ps("ps_tp", [P, 2, TF, P])
        ps_gram = ps("ps_gram", [P, 2, gb, GS, Q])
        ps_h1 = ps("ps_h1", [P, m1, P])
        ps_h2 = ps("ps_h2", [P, 512])

        idx_in = sem("idx_in")
        dense_in = sem("dense_in")
        w1_in = sem("w1_in")
        wd_in = sem("wd_in")
        w2_in = sem("w2_in")
        vec_in = sem("vec_in")
        vec_tp = sem("vec_tp")
        vec_ready = sem("vec_ready")
        ident_zero = sem("ident_zero")
        ident_ready = sem("ident_ready")
        w1_zero = sem("w1_zero")
        pad_zero = sem("pad_zero")
        wd_ready = sem("wd_ready")
        rows_in = [[sem(f"rows_in_{t}_{k}") for k in range(n_tg)] for t in range(nt)]
        tp_done = sem("tp_done")
        feat_dve = sem("feat_dve")
        feat_act = sem("feat_act")
        gram_done = sem("gram_done")
        pairs_dve = sem("pairs_dve")
        pairs_act = sem("pairs_act")
        h1_mm = sem("h1_mm")
        h1_ready = sem("h1_ready")
        h2_mm = sem("h2_mm")
        h2_ready = sem("h2_ready")
        y_mm = sem("y_mm")
        y_ready = sem("y_ready")
        out_done = sem("out_done")

        def group_features(k):
            return range(TF * k, min(TF * k + TF, NF))

        def feat_by_dve(s):
            return s // 2 + 1 if s >= 0 else 0

        def feat_by_act(s):
            return (s + 1) // 2

        block = ctx.enter_context(nc.Block())

        @block.sync
        def _(sp):
            sp.dma_start(idx[:, :], ids.rearrange("(p t) f -> p (t f)", t=nt)).then_inc(idx_in, 16)
            sp.dma_start(dense_sb[:, :, :], dense.rearrange("(p t) d -> p t d", t=nt)).then_inc(dense_in, 16)
            sp.dma_start(vec_rows[0:m1, :], b1.rearrange("(m p) -> m p", p=P)).then_inc(vec_in, 16)
            sp.dma_start(vec_rows[m1:m1 + m2, :], b2.rearrange("(m p) -> m p", p=P)).then_inc(vec_in, 16)
            sp.dma_start(vec_rows[m1 + m2:, :], w3.rearrange("(m p) n -> m (p n)", p=P)).then_inc(vec_in, 16)
            sp.wait_ge(w1_zero, 1)
            row = P
            for i in range(NSLOT):
                n = NF - 1 - i
                p0 = Q * (i % 4) + i + 1
                sp.dma_start(w1_pair[p0:p0 + n, i // 4, :], w1[row:row + n, :]).then_inc(w1_in, 16)
                row += n
            sp.dma_start(w1_dense[:, 0, :], w1[0:P, :]).then_inc(wd_in, 16)
            sp.dma_start(w1_dense[:, 1, :], w1[row:row + P, :]).then_inc(wd_in, 16)
            sp.dma_start(w2_sb[:, :, :], w2.rearrange("(m p) n -> p m n", p=P)).then_inc(w2_in, 16)
            sp.wait_ge(y_ready, nt)
            sp.dma_start(out.rearrange("(p t) o -> p (t o)", t=nt), y_sb[:, :]).then_inc(out_done, 16)
            sp.wait_ge(out_done, 16)

        @block.gpsimd
        def _(pool):
            nc.gpsimd.memset(ident[:, :], 0.0).then_inc(ident_zero, 1)
            pool.wait_ge(ident_zero, 1)
            nc.gpsimd.affine_select(out=ident[:, :], in_=ident[:, :], compare_op=ALU.not_equal, fill=1.0,
                                    base=0, pattern=[[-1, P]], channel_multiplier=1).then_inc(ident_ready, 1)
            pool.wait_ge(idx_in, 16)
            for t in range(nt):
                for f in range(NSPARSE):
                    c = t * NSPARSE + f
                    pool.indirect_dma_start(
                        rows[:, t, f, :], None, tables[f][:, :],
                        bass.IndirectOffsetOnAxis(ap=idx[:, c:c + 1], axis=0),
                    ).then_inc(rows_in[t][(f + 1) // TF], 16)

        @block.tensor
        def _(pe):
            pe.wait_ge(ident_ready, 1)
            pe.wait_ge(vec_in, 48)
            nc.tensor.transpose(ps_h2[:, 0:m1 + 2 * m2], vec_rows[:, :],
                                ident[0:m1 + 2 * m2, 0:m1 + 2 * m2]).then_inc(vec_tp, 1)
            for t in range(nt):
                for k in range(n_tg):
                    s = t * n_tg + k
                    if s == 0:
                        pe.wait_ge(dense_in, 16)
                    pe.wait_ge(rows_in[t][k], 16 * sum(n > 0 for n in group_features(k)))
                    if s >= 2:
                        if s % 2 == 0:
                            pe.wait_ge(feat_dve, feat_by_dve(s - 2))
                        else:
                            pe.wait_ge(feat_act, feat_by_act(s - 2))
                    for n in group_features(k):
                        src = dense_sb[:, t, :] if n == 0 else rows[:, t, n - 1, :]
                        last = nc.tensor.transpose(ps_tp[:, s % 2, n % TF, :], src, ident[:, :])
                    last.then_inc(tp_done, 1)
                pe.wait_ge(feat_dve, feat_by_dve(t * n_tg + n_tg - 1))
                pe.wait_ge(feat_act, feat_by_act(t * n_tg + n_tg - 1))
                if t == 0:
                    pe.wait_ge(pad_zero, 2)
                for a in range(n_gb):
                    u = t * n_gb + a
                    if u >= 2:
                        pe.wait_ge(pairs_dve, u - 1)
                        pe.wait_ge(pairs_act, u - 1)
                    for q in range(gb):
                        p0 = GS * (a * gb + q)
                        feats = feat_T[:, t % 2, p0:p0 + GS, :]
                        last = nc.tensor.matmul(ps_gram[:, u % 2, q, :, 0:NSLOT],
                                                feats.rearrange("d g n -> d (g n)"),
                                                feats[:, :, 0:NSLOT], start=True, stop=True)
                    last.then_inc(gram_done, 1)
                if t == 0:
                    pe.wait_ge(w1_in, 16 * NSLOT)
                    pe.wait_ge(wd_ready, 1)
                if t >= 1:
                    pe.wait_ge(h1_ready, m1 * t)
                for m in range(m1):
                    nc.tensor.matmul(ps_h1[:, m, :], w1_dense[:, 2, m * P:(m + 1) * P],
                                     feat_T[:, t % 2, :, 0], start=True, stop=False)
                    if m == 0:
                        pe.wait_ge(pairs_dve, n_gb * (t + 1))
                        pe.wait_ge(pairs_act, n_gb * (t + 1))
                    for c in range(nc_pair):
                        last = nc.tensor.matmul(ps_h1[:, m, :], w1_pair[:, c, m * P:(m + 1) * P],
                                                pairs[:, t % 2, c, :], start=False, stop=(c == nc_pair - 1))
                last.then_inc(h1_mm, 1)
                if t == 0:
                    pe.wait_ge(w2_in, 16)
                    pe.wait_ge(vec_ready, 1)
                pe.wait_ge(h1_ready, m1 * (t + 1))
                if t >= 1:
                    pe.wait_ge(y_ready, t)
                for m in range(m2):
                    for c in range(m1):
                        last = nc.tensor.matmul(ps_h2[:, m * P:(m + 1) * P], w2_sb[:, c, m * P:(m + 1) * P],
                                                h1_T[:, c, :], start=(c == 0), stop=(c == m1 - 1))
                last.then_inc(h2_mm, 1)
                pe.wait_ge(h2_ready, m2 * (t + 1))
                for c in range(m2):
                    last = nc.tensor.matmul(ps_h2[:, h2n:h2n + 1], h2_T[:, c, :], w3_sb[:, c:c + 1],
                                            start=(c == 0), stop=(c == m2 - 1))
                last.then_inc(y_mm, 1)

        def pick(copy, t, a, g, r):
            u = t * n_gb + a
            nch = len(range(r, NSLOT, 4))
            src = ps_gram[Q * g:Q * g + Q, u % 2, :, g, r:NSLOT:4].rearrange("j q c -> j c q")
            p0 = GS * a * gb + g
            dst = pairs[Q * r:Q * r + Q, t % 2, 0:nch, p0:p0 + GS * (gb - 1) + 1:GS]
            return copy(dst, src)

        @block.vector
        def _(dve):
            nc.vector.memset(w1_pair[:, :, :], 0.0).then_inc(w1_zero, 1)
            nc.vector.memset(feat_T[:, :, :, NF:Q], 0.0).then_inc(pad_zero, 1)
            nc.vector.memset(pairs[Q * (NSLOT - 4 * (nc_pair - 1)):P, :, nc_pair - 1, :], 0.0).then_inc(pad_zero, 1)
            dve.wait_ge(vec_tp, 1)
            nc.vector.tensor_copy(vec_T[:, :], ps_h2[:, 0:m1 + 2 * m2]).then_inc(vec_ready, 1)
            dve.wait_ge(wd_in, 32)
            nc.vector.tensor_tensor(w1_dense[:, 2, :], w1_dense[:, 0, :], w1_dense[:, 1, :],
                                    ALU.add).then_inc(wd_ready, 1)
            for t in range(nt):
                for k in range(n_tg):
                    s = t * n_tg + k
                    if s % 2 == 0:
                        dve.wait_ge(tp_done, s + 1)
                        if t >= 2:
                            dve.wait_ge(h1_mm, t - 1)
                        cnt = len(group_features(k))
                        nc.vector.tensor_copy(
                            feat_T[:, t % 2, :, TF * k:TF * k + cnt].rearrange("d p n -> d n p"),
                            ps_tp[:, 0, 0:cnt, :]).then_inc(feat_dve, 1)
                if t >= 2:
                    dve.wait_ge(h1_mm, t - 1)
                for a in range(n_gb):
                    dve.wait_ge(gram_done, t * n_gb + a + 1)
                    for g in range(GS // 2):
                        for r in range(4):
                            last = pick(nc.vector.tensor_copy, t, a, g, r)
                    last.then_inc(pairs_dve, 1)
                if t == 0:
                    dve.wait_ge(vec_ready, 1)
                dve.wait_ge(h2_mm, t + 1)
                if t >= 1:
                    dve.wait_ge(y_mm, t)
                for m in range(m2):
                    nc.vector.tensor_scalar(h2_T[:, m, :], ps_h2[:, m * P:(m + 1) * P], b2_sb[:, m:m + 1], 0.0,
                                            ALU.add, ALU.max).then_inc(h2_ready, 1)
                dve.wait_ge(y_mm, t + 1)
                nc.vector.tensor_copy(y_sb[:, t:t + 1], ps_h2[:, h2n:h2n + 1]).then_inc(y_ready, 1)

        @block.scalar
        def _(act):
            for t in range(nt):
                for k in range(n_tg):
                    s = t * n_tg + k
                    if s % 2 == 1:
                        act.wait_ge(tp_done, s + 1)
                        if t >= 2:
                            act.wait_ge(h1_mm, t - 1)
                        cnt = len(group_features(k))
                        nc.scalar.copy(
                            feat_T[:, t % 2, :, TF * k:TF * k + cnt].rearrange("d p n -> d n p"),
                            ps_tp[:, 1, 0:cnt, :]).then_inc(feat_act, 1)
                if t >= 2:
                    act.wait_ge(h1_mm, t - 1)
                for a in range(n_gb):
                    act.wait_ge(gram_done, t * n_gb + a + 1)
                    for g in range(GS // 2, GS):
                        for r in range(4):
                            last = pick(nc.scalar.copy, t, a, g, r)
                    last.then_inc(pairs_act, 1)
                if t == 0:
                    act.wait_ge(vec_ready, 1)
                act.wait_ge(h1_mm, t + 1)
                if t >= 1:
                    act.wait_ge(h2_mm, t)
                for m in range(m1):
                    nc.scalar.activation(h1_T[:, m, :], ps_h1[:, m, :], ACT.Relu,
                                         bias=b1_sb[:, m:m + 1]).then_inc(h1_ready, 1)


TABLES = [f"tbl_{f}" for f in range(NSPARSE)]
INPUTS = ["r_dense_features", "ids"] + TABLES + ["W_top1", "b_top1", "W_top2", "b_top2", "W_top3"]


def kernel(**inputs):
    import numpy as np
    import concourse.bacc as bacc
    from concourse.bass_utils import run_bass_kernel_spmd

    nc = bacc.Bacc("TRN2", target_bir_lowering=False, num_devices=1)
    arrays, ap = {}, {}
    for name in INPUTS:
        a = np.ascontiguousarray(inputs[name])
        arrays[f"in_{name}"] = a
        ap[name] = nc.dram_tensor(f"in_{name}", a.shape, mybir.dt.from_np(a.dtype), kind="ExternalInput").ap()
    out = nc.dram_tensor("out_y", (inputs["ids"].shape[0], 1), F32, kind="ExternalOutput").ap()
    dlrm_tower(nc, ap["r_dense_features"], ap["ids"], [ap[n] for n in TABLES],
               ap["W_top1"], ap["b_top1"], ap["W_top2"], ap["b_top2"], ap["W_top3"], out)
    r = run_bass_kernel_spmd(nc, [arrays], core_ids=[0])
    return r.results[0]["out_y"]
```

```python
from contextlib import ExitStack

import concourse.bass as bass
from concourse import mybir

F32 = mybir.dt.float32
F32R = mybir.dt.float32r
I32 = mybir.dt.int32
ALU = mybir.AluOpType
ACT = mybir.ActivationFunctionType

P = 128
Q = 32
NSPARSE = 26
NF = NSPARSE + 1
NDIRECT = 3
NSLOT = NF - NDIRECT
GS = 4
GB = 8
HS = 2

ONEHOT = (9, 10, 14, 16, 18, 20)
FETCH_RUNS = (((23, 24, 25, 26),), ((17, 19, 21), (22,)), ((8, 11), (12, 13)), ((15,),), ((4, 5, 6, 7),),
              ((0, 1, 2, 3),))
GROUPS_AFTER = ((0, 1), (2, 3), (4, 5))
DIRECT_GROUP = 3

FETCH_GROUPS = tuple(tuple(n for run in group for n in run) for group in FETCH_RUNS)
FETCHED = tuple(n for group in FETCH_GROUPS for n in group if n > 0)
DIRECT_PAIRS = tuple((i, j) for i in range(NSLOT, NF) for j in range(i + 1, NF))


def dlrm_tower(nc, dense, ids, ids_onehot, tables, w1, b1, w2, b2, w3, out):
    batch, _ = ids.shape
    nt = batch // P
    h1n = w1.shape[1]
    h2n = w2.shape[1]
    m1 = h1n // P
    m2 = h2n // P
    nc_pair = NSLOT // 4
    n_fg = len(FETCH_GROUPS)
    n_gb = P // GS // GB
    gram_rows = Q * (GS - 1) + NF
    direct_row = Q * 3 + NF
    short = tables[ONEHOT[0] - 1].shape[0]
    n_full = short // P
    n_rest = short - n_full * P
    n_oc = n_full + 1
    nh = len(ONEHOT)
    n_phase = nh // HS
    n_stage, n_parts = 2, 2 * HS
    assert sorted(ONEHOT + FETCHED) == list(range(1, NF)) and n_rest > 0 and NSLOT % 4 == 0
    assert all(tables[n - 1].shape[0] == short for n in ONEHOT)
    assert all(n in FETCH_GROUPS[0] for n in range(NSLOT, NF)) and batch == 512

    with ExitStack() as ctx:
        def sb(name, shape, dt=F32):
            return ctx.enter_context(nc.sbuf_tensor(name, shape, dt))

        def ps(name, shape):
            return ctx.enter_context(nc.psum_tensor(name, shape, F32))

        def sem(name):
            return ctx.enter_context(nc.semaphore(name))

        idx = sb("idx", [P, nt * NSPARSE], I32)
        ident = sb("ident", [P, P])
        row_of = sb("row_of", [P, n_oc])
        ids_all = sb("ids_all", [P, 2, HS * batch], I32)
        onehot = sb("onehot", [P, n_oc, HS, batch], F32R)
        stage = sb("stage", [P, n_stage, n_oc * P])
        tbl_hi = sb("tbl_hi", [P, n_parts, n_oc * P], F32R)
        tbl_lo = sb("tbl_lo", [P, n_parts, n_oc * P], F32R)
        dense_sb = sb("dense_sb", [P, nt, P])
        rows = sb("rows", [P, 2, len(FETCHED), P])
        feat_T = sb("feat_T", [P, nt, P, Q])
        products = sb("products", [P, P])
        direct = sb("direct", [P, P])
        pairs = sb("pairs", [P, 2, nc_pair, P])
        w1_pair = sb("w1_pair", [P, nc_pair, h1n])
        w1_dense = sb("w1_dense", [P, 2, h1n])
        w2_sb = sb("w2_sb", [P, m1, h2n])
        vec_rows = sb("vec_rows", [m1 + 2 * m2, P])
        vec_T = sb("vec_T", [P, m1 + 2 * m2])
        b1_sb = vec_T[:, 0:m1]
        b2_sb = vec_T[:, m1:m1 + m2]
        w3_sb = vec_T[:, m1 + m2:m1 + 2 * m2]
        h1_T = sb("h1_T", [P, m1, P])
        h2_T = sb("h2_T", [P, m2, P])
        y_sb = sb("y_sb", [P, nt])

        ps_feat = ps("ps_feat", [P, 2, 4, P])
        ps_gram = ps("ps_gram", [P, 2, GB, GS, Q])
        ps_onehot = ps_gram[:, :, :, :, :].rearrange("p v (h q) g i -> p v h (q g i)", h=HS)
        ps_h1 = ps("ps_h1", [P, m1, P])
        ps_h2 = ps("ps_h2", [P, 512])

        idx_in = sem("idx_in")
        ids_in = [sem(f"ids_in_{v}") for v in range(n_phase)]
        dense_in = sem("dense_in")
        table_in = [sem(f"table_in_{h}") for h in range(nh)]
        w1_in = sem("w1_in")
        wd_in = sem("wd_in")
        w2_in = sem("w2_in")
        vec_in = sem("vec_in")
        vec_tp = sem("vec_tp")
        vec_ready = sem("vec_ready")
        ident_zero = sem("ident_zero")
        ident_ready = sem("ident_ready")
        row_ready = sem("row_ready")
        stage_zero = sem("stage_zero")
        w1_zero = sem("w1_zero")
        pad_zero = sem("pad_zero")
        direct_zero = sem("direct_zero")
        wd_ready = sem("wd_ready")
        hi_ready = sem("hi_ready")
        lo_ready = sem("lo_ready")
        onehot_ready = sem("onehot_ready")
        onehot_used = sem("onehot_used")
        onehot_dve = sem("onehot_dve")
        onehot_act = sem("onehot_act")
        rows_in = [[sem(f"rows_in_{t}_{k}") for k in range(n_fg)] for t in range(nt)]
        direct_mul = sem("direct_mul")
        direct_ready = sem("direct_ready")
        bank_full = [sem("bank0_full"), sem("bank1_full")]
        bank_copied = [sem("bank0_copied_by_dve"), sem("bank1_copied_by_act")]
        gram_done = sem("gram_done")
        pairs_dve = sem("pairs_dve")
        pairs_act = sem("pairs_act")
        h1_mm = sem("h1_mm")
        h1_ready = sem("h1_ready")
        h2_mm = sem("h2_mm")
        h2_ready = sem("h2_ready")
        y_mm = sem("y_mm")
        y_ready = sem("y_ready")
        out_done = sem("out_done")

        def fetched_count(k):
            return sum(n > 0 for n in FETCH_GROUPS[k])

        def rows_slot(n):
            return FETCHED.index(n)

        def bank_use(t, k):
            return len(range(k % 2, n_fg, 2)) * t + k // 2

        def copy_group(copy, t, k):
            at = 0
            for run in FETCH_RUNS[k]:
                step = run[1] - run[0] if len(run) > 1 else 1
                last = copy(feat_T[:, t, :, run[0]:run[-1] + 1:step].rearrange("d p n -> d n p"),
                            ps_feat[:, k % 2, at:at + len(run), :])
                at += len(run)
            return last

        def copy_onehot(copy, v, e):
            return copy(feat_T[:, :, :, ONEHOT[HS * v + e]],
                        ps_onehot[:, v % 2, e, :].rearrange("d (t p) -> d t p", p=P))

        def pick(copy, u, g, r):
            t, a = divmod(u, n_gb)
            src = ps_gram[Q * g:Q * g + NF, u % 2, :, g, r:NSLOT:4].rearrange("j q c -> j c q")
            p0 = GS * GB * a + g
            return copy(pairs[Q * r:Q * r + NF, t % 2, :, p0:p0 + GS * (GB - 1) + 1:GS], src)

        block = ctx.enter_context(nc.Block())

        @block.sync
        def _(sp):
            def load_ids(v):
                sp.dma_start(ids_all[:, v % 2, :], ids_onehot[v:v + 1, :].to_broadcast([P, HS * batch])
                             ).then_inc(ids_in[v], 16)

            sp.dma_start(idx[:, :], ids.rearrange("(p t) f -> p (t f)", t=nt)).then_inc(idx_in, 16)
            load_ids(0)
            sp.wait_ge(stage_zero, 1)
            for h, n in enumerate(ONEHOT):
                if h >= n_stage:
                    sp.wait_ge(lo_ready, h - n_stage + 1)
                tbl = tables[n - 1]
                sp.dma_start(stage[:, h % n_stage, 0:n_full * P],
                             tbl[0:n_full * P, :].rearrange("(p c) d -> p (c d)", p=P)).then_inc(table_in[h], 16)
                sp.dma_start(stage[0:n_rest, h % n_stage, n_full * P:],
                             tbl[n_full * P:, :]).then_inc(table_in[h], 16)
                if h == 1:
                    load_ids(1)
                    sp.dma_start(dense_sb[:, :, :], dense.rearrange("(p t) d -> p t d", t=nt)).then_inc(dense_in, 16)
                if h % HS == 1 and h // HS + 1 >= 2 and h // HS + 1 < n_phase:
                    v = h // HS + 1
                    sp.wait_ge(onehot_ready, n_oc * (v - 1))
                    load_ids(v)
            sp.dma_start(vec_rows[0:m1, :], b1.rearrange("(m p) -> m p", p=P)).then_inc(vec_in, 16)
            sp.dma_start(vec_rows[m1:m1 + m2, :], b2.rearrange("(m p) -> m p", p=P)).then_inc(vec_in, 16)
            sp.dma_start(vec_rows[m1 + m2:, :], w3.rearrange("(m p) n -> m (p n)", p=P)).then_inc(vec_in, 16)
            sp.wait_ge(w1_zero, 1)
            row = P
            for i in range(NSLOT):
                n = NF - 1 - i
                p0 = Q * (i % 4) + i + 1
                sp.dma_start(w1_pair[p0:p0 + n, i // 4, :], w1[row:row + n, :]).then_inc(w1_in, 16)
                row += n
            n = len(DIRECT_PAIRS)
            sp.dma_start(w1_pair[direct_row:direct_row + n, nc_pair - 1, :], w1[row:row + n, :]).then_inc(w1_in, 16)
            row += n
            sp.dma_start(w1_dense[:, 0, :], w1[0:P, :]).then_inc(wd_in, 16)
            sp.dma_start(w1_dense[:, 1, :], w1[row:row + P, :]).then_inc(wd_in, 16)
            sp.dma_start(w2_sb[:, :, :], w2.rearrange("(m p) n -> p m n", p=P)).then_inc(w2_in, 16)
            sp.wait_ge(y_ready, nt)
            sp.dma_start(out.rearrange("(p t) o -> p (t o)", t=nt), y_sb[:, :]).then_inc(out_done, 16)
            sp.wait_ge(out_done, 16)

        @block.gpsimd
        def _(pool):
            nc.gpsimd.iota(row_of[:, 0:n_full], [[1, n_full]], base=0, channel_multiplier=n_full,
                           allow_small_or_imprecise_dtypes=True).then_inc(row_ready, 1)
            nc.gpsimd.iota(row_of[:, n_full:n_oc], [[1, 1]], base=n_full * P, channel_multiplier=1,
                           allow_small_or_imprecise_dtypes=True).then_inc(row_ready, 1)
            nc.gpsimd.memset(ident[:, :], 0.0).then_inc(ident_zero, 1)
            pool.wait_ge(ident_zero, 1)
            nc.gpsimd.affine_select(out=ident[:, :], in_=ident[:, :], compare_op=ALU.not_equal, fill=1.0,
                                    base=0, pattern=[[-1, P]], channel_multiplier=1).then_inc(ident_ready, 1)
            pool.wait_ge(idx_in, 16)
            for t in range(nt):
                for k, group in enumerate(FETCH_GROUPS):
                    if t >= 2:
                        pool.wait_ge(bank_full[k % 2], bank_use(t - 2, k) + 1)
                    if t >= 2 and k == 0:
                        pool.wait_ge(direct_ready, len(DIRECT_PAIRS) * (t - 1))
                    for n in group:
                        if n == 0:
                            continue
                        c = t * NSPARSE + n - 1
                        pool.indirect_dma_start(
                            rows[:, t % 2, rows_slot(n), :], None, tables[n - 1][:, :],
                            bass.IndirectOffsetOnAxis(ap=idx[:, c:c + 1], axis=0),
                        ).then_inc(rows_in[t][k], 16)

        @block.tensor
        def _(pe):
            def lookup_onehot(v):
                if v >= 2:
                    pe.wait_ge(onehot_dve, v - 1)
                    pe.wait_ge(onehot_act, v - 1)
                for c in range(n_oc):
                    pe.wait_ge(onehot_ready, n_oc * v + c + 1)
                    for e in range(HS):
                        h = HS * v + e
                        if c == 0:
                            pe.wait_ge(hi_ready, h + 1)
                            pe.wait_ge(lo_ready, h + 1)
                        for part in (tbl_hi, tbl_lo):
                            last = nc.tensor.matmul(
                                ps_onehot[:, v % 2, e, :], part[:, h % n_parts, c * P:(c + 1) * P],
                                onehot[:, c, e, :], start=(c == 0 and part is tbl_hi),
                                stop=(c == n_oc - 1 and part is tbl_lo))
                    last.then_inc(onehot_used, 1)

            def transpose_group(t, k):
                if t == 0 and 0 in FETCH_GROUPS[k]:
                    pe.wait_ge(dense_in, 16)
                pe.wait_ge(rows_in[t][k], 16 * fetched_count(k))
                if bank_use(t, k):
                    pe.wait_ge(bank_copied[k % 2], bank_use(t, k))
                for at, n in enumerate(FETCH_GROUPS[k]):
                    src = dense_sb[:, t, :] if n == 0 else rows[:, t % 2, rows_slot(n), :]
                    last = nc.tensor.transpose(ps_feat[:, k % 2, at, :], src, ident[:, :])
                if k == DIRECT_GROUP:
                    pe.wait_ge(direct_ready, len(DIRECT_PAIRS) * (t + 1))
                    last = nc.tensor.transpose(ps_feat[:, k % 2, 3, :], direct[:, :], ident[:, :])
                last.then_inc(bank_full[k % 2], 1)

            def gram(t):
                for k in (n_fg - 2, n_fg - 1):
                    pe.wait_ge(bank_copied[k % 2], bank_use(t, k) + 1)
                if t == 0:
                    pe.wait_ge(pad_zero, 2)
                    pe.wait_ge(onehot_dve, n_phase)
                    pe.wait_ge(onehot_act, n_phase)
                for a in range(n_gb):
                    u = t * n_gb + a
                    if u >= 2:
                        pe.wait_ge(pairs_dve, u - 1)
                        pe.wait_ge(pairs_act, u - 1)
                    for q in range(GB):
                        p0 = GS * (a * GB + q)
                        feats = feat_T[:, t, p0:p0 + GS, :]
                        last = nc.tensor.matmul(ps_gram[0:gram_rows, u % 2, q, :, 0:NSLOT],
                                                feats.rearrange("d g n -> d (g n)")[:, 0:gram_rows],
                                                feats[:, :, 0:NSLOT], start=True, stop=True)
                    last.then_inc(gram_done, 1)

            def layer_1(t):
                if t == 0:
                    pe.wait_ge(w1_in, 16 * (NSLOT + 1))
                    pe.wait_ge(wd_ready, 1)
                else:
                    pe.wait_ge(h1_ready, t)
                for m in range(m1):
                    nc.tensor.matmul(ps_h1[:, m, :], w1_dense[:, 0, m * P:(m + 1) * P], feat_T[:, t, :, 0],
                                     start=True, stop=False)
                    if m == 0:
                        pe.wait_ge(pairs_dve, n_gb * (t + 1))
                        pe.wait_ge(pairs_act, n_gb * (t + 1))
                    for c in range(nc_pair):
                        last = nc.tensor.matmul(ps_h1[:, m, :], w1_pair[:, c, m * P:(m + 1) * P],
                                                pairs[:, t % 2, c, :], start=False, stop=(c == nc_pair - 1))
                    if m == m1 - 1:
                        last.then_inc(h1_mm, 1)
                    if m == 0 and t >= 1:
                        layer_3(t - 1)
                    if t + 1 < nt and m < len(GROUPS_AFTER):
                        for k in GROUPS_AFTER[m]:
                            transpose_group(t + 1, k)

            def layer_2(t):
                if t == 0:
                    pe.wait_ge(w2_in, 16)
                    pe.wait_ge(vec_ready, 1)
                else:
                    pe.wait_ge(y_ready, t)
                pe.wait_ge(h1_ready, t + 1)
                for m in range(m2):
                    for c in range(m1):
                        last = nc.tensor.matmul(ps_h2[:, m * P:(m + 1) * P], w2_sb[:, c, m * P:(m + 1) * P],
                                                h1_T[:, c, :], start=(c == 0), stop=(c == m1 - 1))
                last.then_inc(h2_mm, 1)

            def layer_3(t):
                pe.wait_ge(h2_ready, t + 1)
                for c in range(m2):
                    last = nc.tensor.matmul(ps_h2[:, h2n:h2n + 1], h2_T[:, c, :], w3_sb[:, c:c + 1],
                                            start=(c == 0), stop=(c == m2 - 1))
                last.then_inc(y_mm, 1)

            for v in range(n_phase):
                lookup_onehot(v)
            pe.wait_ge(ident_ready, 1)
            pe.wait_ge(vec_in, 48)
            nc.tensor.transpose(ps_h2[:, 0:m1 + 2 * m2], vec_rows[:, :],
                                ident[0:m1 + 2 * m2, 0:m1 + 2 * m2]).then_inc(vec_tp, 1)
            for k in range(n_fg):
                transpose_group(0, k)
            for t in range(nt):
                gram(t)
                if t >= 1:
                    layer_2(t - 1)
                layer_1(t)
            layer_2(nt - 1)
            layer_3(nt - 1)

        @block.vector
        def _(dve):
            def make_onehot(v, c):
                if c == 0:
                    dve.wait_ge(ids_in[v], 16)
                    if v == 0:
                        dve.wait_ge(row_ready, 2)
                if v > 0:
                    dve.wait_ge(onehot_used, n_oc * (v - 1) + c + 1)
                nc.vector.tensor_scalar(onehot[:, c, :, :].rearrange("p h b -> p (h b)"),
                                        ids_all[:, v % 2, :], row_of[:, c:c + 1], None,
                                        ALU.is_equal).then_inc(onehot_ready, 1)

            def copy_onehot_first(v):
                dve.wait_ge(onehot_used, n_oc * (v + 1))
                copy_onehot(nc.vector.tensor_copy, v, 0).then_inc(onehot_dve, 1)

            def direct_pairs(t):
                dve.wait_ge(rows_in[t][0], 16 * fetched_count(0))
                for e, (i, j) in enumerate(DIRECT_PAIRS):
                    if t + e > 0:
                        dve.wait_ge(direct_ready, len(DIRECT_PAIRS) * t + e)
                    nc.vector.tensor_tensor_reduce(
                        out=products[:, :], in0=rows[:, t % 2, rows_slot(i), :], in1=rows[:, t % 2, rows_slot(j), :],
                        scale=1.0, scalar=0.0, op0=ALU.mult, op1=ALU.add,
                        accum_out=direct[:, direct_row + e:direct_row + e + 1]).then_inc(direct_ready, 1)

            def copy_bank0(t, groups):
                for k in groups:
                    if k == DIRECT_GROUP:
                        direct_pairs(t)
                    if k % 2 == 0:
                        dve.wait_ge(bank_full[0], bank_use(t, k) + 1)
                        copy_group(nc.vector.tensor_copy, t, k).then_inc(bank_copied[0], 1)

            def relu_2(t):
                dve.wait_ge(h2_mm, t + 1)
                for m in range(m2):
                    last = nc.vector.tensor_scalar(h2_T[:, m, :], ps_h2[:, m * P:(m + 1) * P],
                                                   b2_sb[:, m:m + 1], 0.0, ALU.add, ALU.max)
                last.then_inc(h2_ready, 1)

            def copy_y(t):
                dve.wait_ge(y_mm, t + 1)
                nc.vector.tensor_copy(y_sb[:, t:t + 1], ps_h2[:, h2n:h2n + 1]).then_inc(y_ready, 1)

            nc.vector.memset(stage[:, :, n_full * P:], 0.0).then_inc(stage_zero, 1)
            nc.vector.memset(direct[:, :], 0.0).then_inc(direct_zero, 1)
            for v in range(n_phase):
                last_chunks = n_oc - 2
                if v == 0:
                    for c in range(n_oc):
                        make_onehot(v, c)
                for e in range(HS):
                    h = HS * v + e
                    dve.wait_ge(hi_ready, h + 1)
                    nc.vector.tensor_tensor(tbl_lo[:, h % n_parts, :], stage[:, h % n_stage, :],
                                            tbl_hi[:, h % n_parts, :].bitcast(F32),
                                            ALU.subtract).then_inc(lo_ready, 1)
                if v >= 1:
                    for c in range(last_chunks):
                        make_onehot(v, c)
                    copy_onehot_first(v - 1)
                    for c in range(last_chunks, n_oc):
                        make_onehot(v, c)
            copy_onehot_first(n_phase - 1)
            dve.wait_ge(vec_tp, 1)
            nc.vector.tensor_copy(vec_T[:, :], ps_h2[:, 0:m1 + 2 * m2]).then_inc(vec_ready, 1)
            dve.wait_ge(direct_zero, 1)
            copy_bank0(0, range(n_fg))
            dve.wait_ge(wd_in, 32)
            nc.vector.tensor_tensor(w1_dense[:, 0, :], w1_dense[:, 0, :], w1_dense[:, 1, :],
                                    ALU.add).then_inc(wd_ready, 1)
            for t in range(nt):
                for u in range(t * n_gb, (t + 1) * n_gb):
                    dve.wait_ge(gram_done, u + 1)
                    for g in range(GS // 2):
                        for r in range(4):
                            last = pick(nc.vector.tensor_copy, u, g, r)
                    last.then_inc(pairs_dve, 1)
                if t >= 1:
                    relu_2(t - 1)
                    copy_y(t - 1)
                if t + 1 < nt:
                    copy_bank0(t + 1, range(n_fg))
            relu_2(nt - 1)
            copy_y(nt - 1)

        @block.scalar
        def _(act):
            def copy_onehot_second(v):
                act.wait_ge(onehot_used, n_oc * (v + 1))
                copy_onehot(nc.scalar.copy, v, 1).then_inc(onehot_act, 1)

            def copy_bank1(t, groups):
                for k in groups:
                    if k % 2 == 1:
                        act.wait_ge(bank_full[1], bank_use(t, k) + 1)
                        if k == DIRECT_GROUP:
                            nc.scalar.copy(pairs[3 * Q:P, t % 2, nc_pair - 1, :], ps_feat[3 * Q:P, 1, 3, :])
                        copy_group(nc.scalar.copy, t, k).then_inc(bank_copied[1], 1)

            def relu_1(t):
                act.wait_ge(h1_mm, t + 1)
                for m in range(m1):
                    last = nc.scalar.activation(h1_T[:, m, :], ps_h1[:, m, :], ACT.Relu, bias=b1_sb[:, m:m + 1])
                last.then_inc(h1_ready, 1)

            act.wait_ge(direct_zero, 1)
            nc.scalar.copy(w1_pair[:, :, :].rearrange("p c n -> p (c n)"),
                           direct[:, 0:1].to_broadcast([P, nc_pair * h1n])).then_inc(w1_zero, 1)
            for v in range(n_phase):
                if v == 1:
                    nc.scalar.copy(feat_T[:, :, :, NF:Q].rearrange("d t p n -> d (t p) n"),
                                   direct[:, 0:1].to_broadcast([P, nt * P * (Q - NF)])
                                   .rearrange("d (b n) -> d b n", n=Q - NF)).then_inc(pad_zero, 1)
                    nc.scalar.copy(pairs[:, :, :, :].rearrange("p u c b -> p (u c b)"),
                                   direct[:, 0:1].to_broadcast([P, 2 * nc_pair * P])).then_inc(pad_zero, 1)
                for e in range(HS):
                    h = HS * v + e
                    act.wait_ge(table_in[h], 32)
                    if v >= 2:
                        act.wait_ge(onehot_used, n_oc * (v - 1))
                    nc.scalar.copy(tbl_hi[:, h % n_parts, :], stage[:, h % n_stage, :]).then_inc(hi_ready, 1)
                if v >= 1:
                    copy_onehot_second(v - 1)
            copy_onehot_second(n_phase - 1)
            act.wait_ge(pad_zero, 2)
            copy_bank1(0, range(n_fg))
            act.wait_ge(vec_ready, 1)
            for t in range(nt):
                for u in range(t * n_gb, (t + 1) * n_gb):
                    act.wait_ge(gram_done, u + 1)
                    for g in range(GS // 2, GS):
                        for r in range(4):
                            last = pick(nc.scalar.copy, u, g, r)
                    last.then_inc(pairs_act, 1)
                if t + 1 < nt:
                    copy_bank1(t + 1, range(n_fg))
                relu_1(t)


TABLES = [f"tbl_{f}" for f in range(NSPARSE)]
INPUTS = ["r_dense_features", "ids"] + TABLES + ["W_top1", "b_top1", "W_top2", "b_top2", "W_top3"]


def kernel(**inputs):
    import numpy as np
    import concourse.bacc as bacc
    from concourse.bass_utils import run_bass_kernel_spmd

    nc = bacc.Bacc("TRN2", target_bir_lowering=False, num_devices=1)
    arrays, ap = {}, {}

    def give(name, a):
        a = np.ascontiguousarray(a)
        arrays[f"in_{name}"] = a
        ap[name] = nc.dram_tensor(f"in_{name}", a.shape, mybir.dt.from_np(a.dtype), kind="ExternalInput").ap()

    for name in INPUTS:
        give(name, inputs[name])
    ids = np.asarray(inputs["ids"])
    ids = ids.reshape(P, -1, NSPARSE)[:, :, [n - 1 for n in ONEHOT]]
    give("ids_onehot", ids.transpose(2, 1, 0).reshape(len(ONEHOT) // HS, -1))
    out = nc.dram_tensor("out_y", (inputs["ids"].shape[0], 1), F32, kind="ExternalOutput").ap()
    dlrm_tower(nc, ap["r_dense_features"], ap["ids"], ap["ids_onehot"], [ap[n] for n in TABLES],
               ap["W_top1"], ap["b_top1"], ap["W_top2"], ap["b_top2"], ap["W_top3"], out)
    r = run_bass_kernel_spmd(nc, [arrays], core_ids=[0])
    return r.results[0]["out_y"]
```

```python
from contextlib import ExitStack

import concourse.bass as bass
from concourse import mybir

F32 = mybir.dt.float32
F32R = mybir.dt.float32r
I32 = mybir.dt.int32
ALU = mybir.AluOpType
ACT = mybir.ActivationFunctionType

P = 128
Q = 32
NSPARSE = 26
NF = NSPARSE + 1
NDIRECT = 7
NSLOT = NF - NDIRECT
GS = 4
GB = 8
HS = 2

ONEHOT = (9, 10, 14, 16, 17, 18, 20)
FETCH_RUNS = (((21, 22, 23, 24),), ((19,), (25, 26)), ((8, 11), (12, 13)), ((0, 1, 2, 3),), ((4, 5, 6, 7),),
              ((15,),))
GROUPS_AFTER_PHASE = ((0, 1), (2, 3), (4, 5), ())
GROUPS_AFTER = ((0,), (1, 2), (3, 4), (5,), ())
GROUPS_AFTER_LAST = ((), (0, 1), (2,), (3,), ())
LAST_GROUPS = (4, 5)
DIRECT_BETWEEN = 3
VEC_PHASE = 1
N_WARM = 6
W1_AHEAD = 6
PADS = Q - NF

FETCH_GROUPS = tuple(tuple(n for run in group for n in run) for group in FETCH_RUNS)
FETCHED = tuple(n for group in FETCH_GROUPS for n in group if n > 0)
DIRECT = (0, *range(NSLOT + 1, NF))
DIRECT_PAIRS = tuple((i, j) for i in DIRECT for j in DIRECT if i < j)


def dlrm_tower(nc, dense, ids, ids_onehot, tables, w1, b1, w2, b2, w3, out):
    batch, _ = ids.shape
    nt = batch // P
    h1n = w1.shape[1]
    h2n = w2.shape[1]
    m1 = h1n // P
    m2 = h2n // P
    nc_pair = NSLOT // 4
    n_fg = len(FETCH_GROUPS)
    n_gb = P // GS // GB
    gram_rows = Q * (GS - 1) + NF
    n_direct = len(DIRECT_PAIRS)
    n_pairs = NF * (NF - 1) // 2
    direct_at = [(nc_pair - 1 - e // (4 * PADS), Q * (e // PADS % 4) + NF + e % PADS) for e in range(n_direct)]
    short = tables[ONEHOT[0] - 1].shape[0]
    n_full = short // P
    n_rest = short - n_full * P
    n_oc = n_full + 1
    nh = len(ONEHOT)
    n_phase = -(-nh // HS)
    n_products = 4
    n_stage, n_hi = 3, 2 * HS
    n_ring = n_oc + 4
    assert sorted(ONEHOT + FETCHED) == list(range(1, NF)) and n_rest > 0 and NSLOT % 4 == 0
    assert all(tables[n - 1].shape[0] == short for n in ONEHOT)
    assert all(n in FETCH_GROUPS[0] + FETCH_GROUPS[1] for n in DIRECT[1:]) and batch == 512
    assert n_direct == 4 * PADS + 1 and m2 == 2

    w1_loads = []
    row = P
    for c in range(nc_pair):
        w1_loads.append([c, slice(0, 3 * Q + 1, Q), row])
        row += 4
    direct_first = {(0, NSLOT + 1): row}
    row += NF - 1 - NSLOT
    for i in range(1, NSLOT + 1):
        p0 = Q * ((i - 1) % 4) + i + 1
        w1_loads.append([(i - 1) // 4, slice(p0, p0 + NF - 1 - i), row])
        row += NF - 1 - i
    direct_first[(NSLOT + 1, NSLOT + 2)] = row
    for e, pair in enumerate(DIRECT_PAIRS):
        c, p0 = direct_at[e]
        if pair in direct_first:
            row = direct_first[pair]
        if pair in direct_first or e % PADS == 0:
            w1_loads.append([c, slice(p0, p0 + 1), row])
        else:
            w1_loads[-1][1] = slice(w1_loads[-1][1].start, p0 + 1)
        row += 1

    with ExitStack() as ctx:
        def sb(name, shape, dt=F32):
            return ctx.enter_context(nc.sbuf_tensor(name, shape, dt))

        def ps(name, shape):
            return ctx.enter_context(nc.psum_tensor(name, shape, F32))

        def sem(name):
            return ctx.enter_context(nc.semaphore(name))

        idx = sb("idx", [P, nt * NSPARSE], I32)
        ident = sb("ident", [P, P])
        one = sb("one", [P, 1])
        row_of = sb("row_of", [P, n_oc])
        ids_all = sb("ids_all", [P, 2, HS * batch], I32)
        onehot = sb("onehot", [P, n_ring, HS, batch], F32R)
        stage = sb("stage", [P, n_stage, n_oc * P])
        tbl_hi = sb("tbl_hi", [P, n_hi, n_oc * P], F32R)
        tbl_lo = sb("tbl_lo", [P, HS, n_oc * P], F32R)
        dense_sb = sb("dense_sb", [P, nt, P])
        rows = sb("rows", [P, 2, len(FETCHED), P])
        feat_T = sb("feat_T", [P, nt, P, Q])
        products = sb("products", [P, n_products, P])
        direct = sb("direct", [P, 2, P])
        pairs = sb("pairs", [P, 2, nc_pair, P])
        w1_pair = sb("w1_pair", [P, nc_pair, h1n])
        w1_dense = sb("w1_dense", [P, 2, h1n])
        w2_sb = sb("w2_sb", [P, m1, h2n])
        vec_rows = sb("vec_rows", [m1 + 2 * m2, P])
        vec_T = sb("vec_T", [P, m1 + 2 * m2])
        b1_sb = vec_T[:, 0:m1]
        b2_sb = vec_T[:, m1:m1 + m2]
        w3_sb = vec_T[:, m1 + m2:m1 + 2 * m2]
        h1_T = sb("h1_T", [P, m1, P])
        h2_T = sb("h2_T", [P, m2, P])
        y_sb = sb("y_sb", [P, nt])

        ps_feat = ps("ps_feat", [P, 2, 4, P])
        ps_gram = ps("ps_gram", [P, 2, GB, GS, Q])
        ps_onehot = ps_gram[:, :, :, :, :].rearrange("p v (h q) g i -> p v h (q g i)", h=HS)
        ps_h1 = ps("ps_h1", [P, m1, P])
        ps_h2 = ps("ps_h2", [P, 512])

        idx_in = sem("idx_in")
        ids_in = [sem(f"ids_in_{v}") for v in range(n_phase)]
        dense_in = sem("dense_in")
        table_in = [sem(f"table_in_{h}") for h in range(nh)]
        w1_in = sem("w1_in")
        wd_in = sem("wd_in")
        w2_in = sem("w2_in")
        vec_in = sem("vec_in")
        vec_tp = sem("vec_tp")
        vec_ready = sem("vec_ready")
        ident_zero = sem("ident_zero")
        ident_ready = sem("ident_ready")
        row_ready = sem("row_ready")
        stage_zero = sem("stage_zero")
        w1_zero = sem("w1_zero")
        pad_zero = sem("pad_zero")
        direct_zero = sem("direct_zero")
        wd_ready = sem("wd_ready")
        hi_ready = sem("hi_ready")
        lo_ready = sem("lo_ready")
        onehot_ready = sem("onehot_ready")
        distance_ready = sem("distance_ready")
        last_chunk_ready = sem("last_chunk_ready")
        one_ready = sem("one_ready")
        onehot_used = sem("onehot_used")
        onehot_copied = sem("onehot_copied")
        rows_in = [[sem(f"rows_in_{t}_{k}") for k in range(n_fg)] for t in range(nt)]
        direct_ready = sem("direct_ready")
        bank_full = [sem("bank0_full"), sem("bank1_full")]
        bank_copied = [sem("bank0_copied"), sem("bank1_copied")]
        gram_done = sem("gram_done")
        pairs_dve = sem("pairs_dve")
        pairs_act = sem("pairs_act")
        h1_mm = sem("h1_mm")
        h1_half = sem("h1_half")
        h1_ready = sem("h1_ready")
        h1_rest = sem("h1_rest")
        h2_mm = sem("h2_mm")
        h2_ready = sem("h2_ready")
        y_mm = sem("y_mm")
        y_ready = sem("y_ready")
        out_done = sem("out_done")

        def phase_tables(v):
            return min(HS, nh - HS * v)

        def fetched_count(k):
            return sum(n > 0 for n in FETCH_GROUPS[k])

        def rows_slot(n):
            return FETCHED.index(n)

        def row_of_sample(t, n):
            return dense_sb[:, t, :] if n == 0 else rows[:, t % 2, rows_slot(n), :]

        def bank_use(t, k):
            return (len(range(k % 2, n_fg, 2)) + 1 - k % 2) * t + k // 2

        def direct_use(t):
            return (len(range(0, n_fg, 2)) + 1) * (t + 1) - 1

        def copy_group(copy, t, k):
            at = 0
            for run in FETCH_RUNS[k]:
                step = run[1] - run[0] if len(run) > 1 else 1
                last = copy(feat_T[:, t, :, run[0]:run[-1] + 1:step].rearrange("d p n -> d n p"),
                            ps_feat[:, k % 2, at:at + len(run), :])
                at += len(run)
            return last

        def copy_onehot(copy, v, e, t0, t1):
            return copy(feat_T[:, t0:t1, :, ONEHOT[HS * v + e]],
                        ps_onehot[:, v % 2, e, t0 * P:t1 * P].rearrange("d (t p) -> d t p", p=P))

        def h1_at(t, m):
            if t == nt - 1 and m >= m1 // 2:
                return ps_feat[:, 0, m - m1 // 2, :]
            return ps_h1[:, m, :]

        def h2_at(t, m):
            if t == nt - 1 and m > 0:
                return ps_feat[:, 1, m, :]
            return ps_h2[:, m * P:(m + 1) * P]

        def pick(copy, u, g, r):
            t, a = divmod(u, n_gb)
            src = ps_gram[Q * g:Q * g + NF, u % 2, :, g, r:NSLOT:4].rearrange("j q c -> j c q")
            p0 = GS * GB * a + g
            return copy(pairs[Q * r:Q * r + NF, t % 2, :, p0:p0 + GS * (GB - 1) + 1:GS], src)

        block = ctx.enter_context(nc.Block())

        @block.sync
        def _(sp):
            def load_ids(v):
                n = phase_tables(v) * batch
                sp.dma_start(ids_all[:, v % 2, 0:n], ids_onehot[:, HS * batch * v:HS * batch * v + n]
                             .to_broadcast([P, n])).then_inc(ids_in[v], 16)

            def load_w1(first, end):
                if first == 0:
                    sp.wait_ge(w1_zero, 1)
                for c, rows_at, row in w1_loads[first:end]:
                    n = len(range(rows_at.start, rows_at.stop, rows_at.step or 1))
                    sp.dma_start(w1_pair[rows_at, c, :], w1[row:row + n, :]).then_inc(w1_in, 16)

            sp.dma_start(idx[:, :], ids.rearrange("(p t) f -> p (t f)", t=nt)).then_inc(idx_in, 16)
            load_ids(0)
            sp.wait_ge(stage_zero, 1)
            for h, n in enumerate(ONEHOT):
                if h >= n_stage:
                    sp.wait_ge(lo_ready, h - n_stage + 1)
                tbl = tables[n - 1]
                sp.dma_start(stage[:, h % n_stage, 0:n_full * P],
                             tbl[0:n_full * P, :].rearrange("(p c) d -> p (c d)", p=P)).then_inc(table_in[h], 16)
                sp.dma_start(stage[0:n_rest, h % n_stage, n_full * P:],
                             tbl[n_full * P:, :]).then_inc(table_in[h], 16)
                if h == 1:
                    load_ids(1)
                    sp.dma_start(dense_sb[:, :, :], dense.rearrange("(p t) d -> p t d", t=nt)).then_inc(dense_in, 16)
                if h % HS == 1 and h // HS + 1 >= 2 and h // HS + 1 < n_phase:
                    v = h // HS + 1
                    sp.wait_ge(onehot_ready, (n_oc - 1) * (v - 1))
                    sp.wait_ge(last_chunk_ready, v - 1)
                    load_ids(v)
                if h == n_stage + 1:
                    sp.dma_start(vec_rows[0:m1, :], b1.rearrange("(m p) -> m p", p=P)).then_inc(vec_in, 16)
                    sp.dma_start(vec_rows[m1:m1 + m2, :], b2.rearrange("(m p) -> m p", p=P)).then_inc(vec_in, 16)
                    sp.dma_start(vec_rows[m1 + m2:, :], w3.rearrange("(m p) n -> m (p n)", p=P)).then_inc(vec_in, 16)
                    load_w1(0, W1_AHEAD)
            load_w1(W1_AHEAD, len(w1_loads))
            sp.dma_start(w1_dense[:, 0, :], w1[0:P, :]).then_inc(wd_in, 16)
            sp.dma_start(w1_dense[:, 1, :], w1[P + n_pairs:, :]).then_inc(wd_in, 16)
            sp.dma_start(w2_sb[:, :, :], w2.rearrange("(m p) n -> p m n", p=P)).then_inc(w2_in, 16)
            sp.wait_ge(y_ready, nt)
            sp.dma_start(out.rearrange("(p t) o -> p (t o)", t=nt), y_sb[:, :]).then_inc(out_done, 16)
            sp.wait_ge(out_done, 16)

        @block.gpsimd
        def _(pool):
            nc.gpsimd.iota(row_of[:, 0:n_full], [[1, n_full]], base=0, channel_multiplier=n_full,
                           allow_small_or_imprecise_dtypes=True).then_inc(row_ready, 1)
            nc.gpsimd.iota(row_of[:, n_full:n_oc], [[1, 1]], base=n_full * P, channel_multiplier=1,
                           allow_small_or_imprecise_dtypes=True).then_inc(row_ready, 1)
            nc.gpsimd.memset(one[:, :], 1.0).then_inc(one_ready, 1)
            nc.gpsimd.memset(ident[:, :], 0.0).then_inc(ident_zero, 1)
            pool.wait_ge(ident_zero, 1)
            nc.gpsimd.affine_select(out=ident[:, :], in_=ident[:, :], compare_op=ALU.not_equal, fill=1.0,
                                    base=0, pattern=[[-1, P]], channel_multiplier=1).then_inc(ident_ready, 1)
            pool.wait_ge(idx_in, 16)
            for t in range(nt):
                for k, group in enumerate(FETCH_GROUPS):
                    if t >= 2:
                        pool.wait_ge(bank_full[k % 2], bank_use(t - 2, k) + 1)
                    if t >= 2 and k == 0:
                        pool.wait_ge(direct_ready, n_direct * (t - 1))
                    for n in group:
                        if n == 0:
                            continue
                        c = t * NSPARSE + n - 1
                        pool.indirect_dma_start(
                            rows[:, t % 2, rows_slot(n), :], None, tables[n - 1][:, :],
                            bass.IndirectOffsetOnAxis(ap=idx[:, c:c + 1], axis=0),
                        ).then_inc(rows_in[t][k], 16)

        @block.tensor
        def _(pe):
            def lookup_onehot(v):
                if v >= 2:
                    pe.wait_ge(onehot_copied, v - 1)
                es = range(phase_tables(v))
                if v == 0:
                    first = range(n_oc - 3)
                    steps = [(e, c) for e in es for c in first] + [(e, c) for c in range(n_oc)[len(first):]
                                                                   for e in es]
                else:
                    steps = [(e, c) for c in range(n_oc) for e in es]
                for part, n_slots, part_ready in ((tbl_hi, n_hi, hi_ready), (tbl_lo, HS, lo_ready)):
                    for e, c in steps:
                        h = HS * v + e
                        if c == 0:
                            pe.wait_ge(part_ready, h + 1)
                        if part is tbl_hi and e == 0:
                            if c < n_oc - 1:
                                pe.wait_ge(onehot_ready, (n_oc - 1) * v + c + 1)
                            else:
                                pe.wait_ge(last_chunk_ready, v + 1)
                        last = nc.tensor.matmul(
                            ps_onehot[:, v % 2, e, :], part[:, h % n_slots, c * P:(c + 1) * P],
                            onehot[:, (n_oc * v + c) % n_ring, e, :], start=(c == 0 and part is tbl_hi),
                            stop=(c == n_oc - 1 and part is tbl_lo))
                        if part is tbl_lo and e == len(es) - 1:
                            last.then_inc(onehot_used, 1)

            def transpose_group(t, k):
                if t == 0 and 0 in FETCH_GROUPS[k]:
                    pe.wait_ge(dense_in, 16)
                pe.wait_ge(rows_in[t][k], 16 * fetched_count(k))
                if bank_use(t, k):
                    pe.wait_ge(bank_copied[k % 2], bank_use(t, k))
                for at, n in enumerate(FETCH_GROUPS[k]):
                    last = nc.tensor.transpose(ps_feat[:, k % 2, at, :], row_of_sample(t, n), ident[:, :])
                last.then_inc(bank_full[k % 2], 1)

            def transpose_direct(t):
                pe.wait_ge(direct_ready, n_direct * (t + 1))
                pe.wait_ge(bank_copied[0], direct_use(t))
                for e in range(2):
                    last = nc.tensor.transpose(ps_feat[:, 0, e, :], direct[:, e, :], ident[:, :])
                last.then_inc(bank_full[0], 1)

            def gram(t):
                if t > 0:
                    transpose_direct(t)
                for k in (n_fg - 2, n_fg - 1):
                    pe.wait_ge(bank_copied[k % 2], bank_use(t, k) + 1)
                if t == 0:
                    pe.wait_ge(pad_zero, 2)
                    pe.wait_ge(onehot_copied, n_phase)
                for a in range(n_gb):
                    u = t * n_gb + a
                    if u == (n_phase - 1) % 2:
                        pe.wait_ge(onehot_copied, n_phase + 1)
                    if u >= 2:
                        pe.wait_ge(pairs_dve, u - 1)
                        pe.wait_ge(pairs_act, u - 1)
                    for q in range(GB):
                        p0 = GS * (a * GB + q)
                        feats = feat_T[:, t, p0:p0 + GS, :]
                        last = nc.tensor.matmul(ps_gram[0:gram_rows, u % 2, q, :, 0:NSLOT],
                                                feats.rearrange("d g n -> d (g n)")[:, 0:gram_rows],
                                                feats[:, :, 1:NSLOT + 1], start=True, stop=True)
                    last.then_inc(gram_done, 1)
                    if t == 0 and a == 0:
                        transpose_direct(t)

            def layer_1(t):
                if t == 0:
                    pe.wait_ge(w1_in, 16 * len(w1_loads))
                    pe.wait_ge(wd_ready, 1)
                else:
                    pe.wait_ge(h1_ready, t)
                if t == nt - 1:
                    pe.wait_ge(bank_copied[0], direct_use(t) + 1)
                for m in range(m1):
                    nc.tensor.matmul(h1_at(t, m), w1_dense[:, 0, m * P:(m + 1) * P], feat_T[:, t, :, 0],
                                     start=(m == 0 or (t == nt - 1 and m == m1 // 2)), stop=False,
                                     skip_group_check=True)
                groups = GROUPS_AFTER_LAST if t + 1 == nt - 1 else GROUPS_AFTER
                if t + 1 < nt:
                    for k in groups[0]:
                        transpose_group(t + 1, k)
                if t == nt - 1:
                    layer_3(t - 1)
                pe.wait_ge(pairs_dve, n_gb * (t + 1))
                pe.wait_ge(pairs_act, n_gb * (t + 1))
                for m in range(m1):
                    for c in range(nc_pair):
                        last = nc.tensor.matmul(h1_at(t, m), w1_pair[:, c, m * P:(m + 1) * P],
                                                pairs[:, t % 2, c, :], start=False, stop=(c == nc_pair - 1),
                                                skip_group_check=True)
                    if m == m1 - 1:
                        last.then_inc(h1_mm, 1)
                    elif t == nt - 1 and m == m1 // 2 - 1:
                        last.then_inc(h1_half, 1)
                    if m == 0 and 1 <= t < nt - 2:
                        layer_3(t - 1)
                    if t + 1 < nt:
                        for k in groups[m + 1]:
                            transpose_group(t + 1, k)

            def layer_2(t):
                if t == 0:
                    pe.wait_ge(w2_in, 16)
                    pe.wait_ge(vec_ready, 1)
                else:
                    pe.wait_ge(y_ready, t)
                pe.wait_ge(h1_ready, t + 1)
                if t < nt - 1:
                    steps = [(m, c) for m in range(m2) for c in range(m1)]
                else:
                    steps = [(m, half * m1 // 2 + c) for half in range(2) for m in range(m2) for c in range(m1 // 2)]
                for m, c in steps:
                    if t == nt - 1 and m == 0 and c == m1 // 2:
                        pe.wait_ge(h1_rest, 1)
                    last = nc.tensor.matmul(h2_at(t, m), w2_sb[:, c, m * P:(m + 1) * P],
                                            h1_T[:, c, :], start=(c == 0), stop=(c == m1 - 1))
                    if c == m1 - 1 and (t == nt - 1 or m == m2 - 1):
                        last.then_inc(h2_mm, 1)

            def layer_3(t):
                pe.wait_ge(h2_ready, t + 1)
                for c in range(m2):
                    last = nc.tensor.matmul(ps_h2[:, h2n:h2n + 1], h2_T[:, c, :], w3_sb[:, c:c + 1],
                                            start=(c == 0), stop=(c == m2 - 1))
                last.then_inc(y_mm, 1)

            pe.wait_ge(direct_zero, 1)
            for _ in range(N_WARM):
                nc.tensor.matmul(ps_h2[:, 0:2 * P], direct[:, 0, :], direct[:, :, :].rearrange("p e c -> p (e c)"),
                                 start=True, stop=True)
            pe.wait_ge(ident_ready, 1)
            for v in range(n_phase):
                lookup_onehot(v)
                if v == VEC_PHASE:
                    pe.wait_ge(vec_in, 48)
                    nc.tensor.transpose(ps_h2[:, 0:m1 + 2 * m2], vec_rows[:, :],
                                        ident[0:m1 + 2 * m2, 0:m1 + 2 * m2]).then_inc(vec_tp, 1)
                for k in GROUPS_AFTER_PHASE[v]:
                    transpose_group(0, k)
            for t in range(nt):
                gram(t)
                if 1 <= t < nt - 1:
                    layer_2(t - 1)
                layer_1(t)
                if t == nt - 2:
                    layer_3(t - 1)
                    transpose_group(nt - 1, LAST_GROUPS[0])
                    layer_2(t)
                    transpose_group(nt - 1, LAST_GROUPS[1])
            layer_2(nt - 1)
            layer_3(nt - 1)

        @block.vector
        def _(dve):
            def make_onehot(v, c):
                if c == 0:
                    dve.wait_ge(ids_in[v], 16)
                    if v == 0:
                        dve.wait_ge(row_ready, 2)
                u = n_oc * v + c
                if u >= n_ring:
                    dve.wait_ge(onehot_used, u - n_ring + 1)
                n = phase_tables(v) * batch
                nc.vector.tensor_scalar(onehot[:, u % n_ring, :, :].rearrange("p h b -> p (h b)")[:, 0:n],
                                        ids_all[:, v % 2, 0:n], row_of[:, c:c + 1], None,
                                        ALU.is_equal).then_inc(onehot_ready, 1)

            def direct_pairs(t, e0, e1):
                if e0 == 0:
                    for k in (0, 1):
                        dve.wait_ge(rows_in[t][k], 16 * fetched_count(k))
                    dve.wait_ge(dense_in, 16)
                for e in range(e0, e1):
                    i, j = DIRECT_PAIRS[e]
                    column = direct_at[e][1]
                    n = n_direct * t + e
                    if n >= n_products:
                        dve.wait_ge(direct_ready, n - n_products + 1)
                    nc.vector.tensor_tensor_reduce(
                        out=products[:, n % n_products, :], in0=row_of_sample(t, i),
                        in1=row_of_sample(t, j),
                        scale=1.0, scalar=0.0, op0=ALU.mult, op1=ALU.add,
                        accum_out=direct[:, e // (4 * PADS), column:column + 1]).then_inc(direct_ready, 1)

            def copy_bank0(t, groups):
                for k in groups:
                    if k % 2 == 0:
                        dve.wait_ge(bank_full[0], bank_use(t, k) + 1)
                        copy_group(nc.vector.tensor_copy, t, k).then_inc(bank_copied[0], 1)

            def relu_2(t):
                if t < nt - 1:
                    dve.wait_ge(h2_mm, t + 1)
                for m in range(m2):
                    if t == nt - 1:
                        dve.wait_ge(h2_mm, t + m + 1)
                    last = nc.vector.tensor_scalar(h2_T[:, m, :], h2_at(t, m),
                                                   b2_sb[:, m:m + 1], 0.0, ALU.add, ALU.max)
                last.then_inc(h2_ready, 1)

            def copy_y(t):
                dve.wait_ge(y_mm, t + 1)
                nc.vector.tensor_copy(y_sb[:, t:t + 1], ps_h2[:, h2n:h2n + 1]).then_inc(y_ready, 1)

            nc.vector.memset(stage[:, :, n_full * P:], 0.0).then_inc(stage_zero, 1)
            nc.vector.memset(direct[:, :, :], 0.0).then_inc(direct_zero, 1)
            for v in range(n_phase):
                for c in range(n_oc - 1):
                    make_onehot(v, c)
                if v == n_phase - 1:
                    direct_pairs(0, 0, n_direct // 2)
                for e in range(phase_tables(v)):
                    h = HS * v + e
                    dve.wait_ge(hi_ready, h + 1)
                    if v >= 1:
                        dve.wait_ge(onehot_used, n_oc * v)
                    nc.vector.tensor_tensor(tbl_lo[:, e, :], stage[:, h % n_stage, :],
                                            tbl_hi[:, h % n_hi, :].bitcast(F32),
                                            ALU.subtract).then_inc(lo_ready, 1)
                if v == VEC_PHASE + 1:
                    dve.wait_ge(vec_tp, 1)
                    nc.vector.tensor_copy(vec_T[:, :], ps_h2[:, 0:m1 + 2 * m2]).then_inc(vec_ready, 1)
            direct_pairs(0, n_direct // 2, n_direct)
            dve.wait_ge(wd_in, 32)
            nc.vector.tensor_tensor(w1_dense[:, 0, :], w1_dense[:, 0, :], w1_dense[:, 1, :],
                                    ALU.add).then_inc(wd_ready, 1)
            for t in range(nt):
                for u in range(t * n_gb, (t + 1) * n_gb):
                    dve.wait_ge(gram_done, u + 1)
                    if u == t * n_gb:
                        dve.wait_ge(bank_copied[0], direct_use(t) + 1)
                    for g in range(GS // 2):
                        for r in range(4):
                            last = pick(nc.vector.tensor_copy, u, g, r)
                    last.then_inc(pairs_dve, 1)
                    if t + 1 < nt - 1:
                        e0 = DIRECT_BETWEEN * (u - t * n_gb)
                        direct_pairs(t + 1, e0, e0 + DIRECT_BETWEEN)
                if 1 <= t < nt - 1:
                    relu_2(t - 1)
                if t + 1 < nt - 1:
                    copy_bank0(t + 1, (0,))
                    if t >= 1:
                        copy_y(t - 1)
                    copy_bank0(t + 1, (2,))
                    direct_pairs(t + 1, n_gb * DIRECT_BETWEEN, n_direct)
                    copy_bank0(t + 1, (4,))
                elif t + 1 == nt - 1:
                    direct_pairs(t + 1, 0, 8)
                    copy_bank0(t + 1, (0,))
                    direct_pairs(t + 1, 8, 15)
                    copy_bank0(t + 1, (2,))
                    direct_pairs(t + 1, 15, n_direct)
                    copy_y(t - 1)
                    copy_bank0(t + 1, (4,))
                    relu_2(t)
            copy_y(nt - 2)
            dve.wait_ge(h1_mm, nt)
            for m in range(m1 // 2, m1):
                last = nc.vector.tensor_scalar(h1_T[:, m, :], h1_at(nt - 1, m), b1_sb[:, m:m + 1], 0.0,
                                               ALU.add, ALU.max)
            last.then_inc(h1_rest, 1)
            relu_2(nt - 1)
            copy_y(nt - 1)

        @block.scalar
        def _(act):
            def make_last_onehot(v):
                u = n_oc * v + n_oc - 1
                n = phase_tables(v) * batch
                chunk = onehot[:, u % n_ring, :, :].rearrange("p h b -> p (h b)")[:, 0:n]
                act.wait_ge(ids_in[v], 16)
                if v == 0:
                    act.wait_ge(row_ready, 2)
                    act.wait_ge(one_ready, 1)
                if u >= n_ring:
                    act.wait_ge(onehot_used, u - n_ring + 1)
                nc.scalar.activation(chunk, ids_all[:, v % 2, 0:n], ACT.Abs, bias=row_of[:, n_oc - 1:n_oc],
                                     scale=-1.0).then_inc(distance_ready, 1)
                act.wait_ge(distance_ready, v + 1)
                nc.scalar.activation(chunk, chunk.bitcast(F32), ACT.Relu, bias=one[:, :],
                                     scale=-1.0).then_inc(last_chunk_ready, 1)

            def copy_onehot_phase(v):
                act.wait_ge(onehot_used, n_oc * (v + 1))
                for e in range(phase_tables(v)):
                    last = copy_onehot(nc.scalar.copy, v, e, 0, nt)
                last.then_inc(onehot_copied, 1)

            def copy_banks(t, groups):
                for k in groups:
                    if k % 2 == 1 or t == 0:
                        act.wait_ge(bank_full[k % 2], bank_use(t, k) + 1)
                        copy_group(nc.scalar.copy, t, k).then_inc(bank_copied[k % 2], 1)

            def relu_1(t):
                if t < nt - 1:
                    act.wait_ge(h1_mm, t + 1)
                else:
                    act.wait_ge(h1_half, 1)
                for m in range(m1 if t < nt - 1 else m1 // 2):
                    last = nc.scalar.activation(h1_T[:, m, :], ps_h1[:, m, :], ACT.Relu, bias=b1_sb[:, m:m + 1])
                last.then_inc(h1_ready, 1)

            act.wait_ge(direct_zero, 1)
            nc.scalar.copy(w1_pair[:, :, :].rearrange("p c n -> p (c n)"),
                           direct[:, 0, 0:1].to_broadcast([P, nc_pair * h1n])).then_inc(w1_zero, 1)
            for v in range(n_phase):
                for e in range(phase_tables(v)):
                    h = HS * v + e
                    act.wait_ge(table_in[h], 32)
                    if v >= 2:
                        act.wait_ge(onehot_used, n_oc * (v - 1))
                    nc.scalar.copy(tbl_hi[:, h % n_hi, :], stage[:, h % n_stage, :]).then_inc(hi_ready, 1)
                make_last_onehot(v)
                if v == 1:
                    nc.scalar.copy(feat_T[:, :, :, NF:Q].rearrange("d t p n -> d (t p) n"),
                                   direct[:, 0, 0:1].to_broadcast([P, nt * P * (Q - NF)])
                                   .rearrange("d (b n) -> d b n", n=Q - NF)).then_inc(pad_zero, 1)
                if v >= 1:
                    copy_onehot_phase(v - 1)
                    copy_banks(0, GROUPS_AFTER_PHASE[v - 1])
                if v == 2:
                    nc.scalar.copy(pairs[:, :, :, :].rearrange("p u c b -> p (u c b)"),
                                   direct[:, 0, 0:1].to_broadcast([P, 2 * nc_pair * P])).then_inc(pad_zero, 1)
            v = n_phase - 1
            act.wait_ge(onehot_used, n_oc * (v + 1))
            copy_onehot(nc.scalar.copy, v, 0, 0, 1).then_inc(onehot_copied, 1)
            copy_onehot(nc.scalar.copy, v, 0, 1, nt).then_inc(onehot_copied, 1)
            act.wait_ge(vec_ready, 1)
            for t in range(nt):
                for u in range(t * n_gb, (t + 1) * n_gb):
                    if u == t * n_gb:
                        act.wait_ge(bank_full[0], direct_use(t) + 1)
                        nc.scalar.copy(pairs[:, t % 2, nc_pair - 1, :], ps_feat[:, 0, 0, :])
                        nc.scalar.copy(pairs[0:Q, t % 2, nc_pair - 2, :], ps_feat[0:Q, 0, 1, :]
                                       ).then_inc(bank_copied[0], 1)
                        act.wait_ge(bank_copied[0], direct_use(t) + 1)
                    act.wait_ge(gram_done, u + 1)
                    for g in range(GS // 2, GS):
                        for r in range(4):
                            last = pick(nc.scalar.copy, u, g, r)
                    last.then_inc(pairs_act, 1)
                if t + 1 < nt - 1:
                    copy_banks(t + 1, range(n_fg))
                elif t + 1 == nt - 1:
                    copy_banks(t + 1, (k for k in range(n_fg) if k not in LAST_GROUPS))
                relu_1(t)
                if t + 1 == nt - 1:
                    copy_banks(t + 1, LAST_GROUPS)


TABLES = [f"tbl_{f}" for f in range(NSPARSE)]
INPUTS = ["r_dense_features", "ids"] + TABLES + ["W_top1", "b_top1", "W_top2", "b_top2", "W_top3"]


def kernel(**inputs):
    import numpy as np
    import concourse.bacc as bacc
    from concourse.bass_utils import run_bass_kernel_spmd

    nc = bacc.Bacc("TRN2", target_bir_lowering=False, num_devices=1)
    arrays, ap = {}, {}

    def give(name, a):
        a = np.ascontiguousarray(a)
        arrays[f"in_{name}"] = a
        ap[name] = nc.dram_tensor(f"in_{name}", a.shape, mybir.dt.from_np(a.dtype), kind="ExternalInput").ap()

    for name in INPUTS:
        give(name, inputs[name])
    ids = np.asarray(inputs["ids"])
    ids = ids.reshape(P, -1, NSPARSE)[:, :, [n - 1 for n in ONEHOT]]
    give("ids_onehot", ids.transpose(2, 1, 0).reshape(1, -1))
    out = nc.dram_tensor("out_y", (inputs["ids"].shape[0], 1), F32, kind="ExternalOutput").ap()
    dlrm_tower(nc, ap["r_dense_features"], ap["ids"], ap["ids_onehot"], [ap[n] for n in TABLES],
               ap["W_top1"], ap["b_top1"], ap["W_top2"], ap["b_top2"], ap["W_top3"], out)
    r = run_bass_kernel_spmd(nc, [arrays], core_ids=[0])
    return r.results[0]["out_y"]
```
